# Optimizing a Trainium2 kernel written in Bass

```python
import numpy as np
import jax
import jax.numpy as jnp

def _softmax(x, axis=-1):
    return jax.nn.softmax(x, axis=axis)

def _gelu(x):
    return jax.nn.gelu(x, approximate=True)

def _silu(x):
    return jax.nn.silu(x)

def _sigmoid(x):
    return jax.nn.sigmoid(x)

def _layernorm(x, axis=-1, eps=1e-05):
    m = jnp.mean(x, axis=axis, keepdims=True)
    v = jnp.var(x, axis=axis, keepdims=True)
    return (x - m) / jnp.sqrt(v + eps)

def _scatter_add(tgt, idx, src, axis=0):
    return tgt.at[idx].add(src)

def _segment_sum(src, seg, n):
    return jax.ops.segment_sum(src, seg, n)
kernel_name = 'mk_adj_preln_d1_adj_r2_7eca2c'

def setup_inputs(seed: int=0):
    np.random.seed(seed)
    _w = jnp.asarray

    def _rec_inputs():
        import jax
        import jax.numpy as jnp
        _gk = jax.random.key(seed)
        x = -0.0002928 + 1 * jax.random.normal(jax.random.fold_in(_gk, 1), (8, 1024, 256), jnp.float32)
        _a = jax.random.bernoulli(jax.random.fold_in(_gk, 2), 0.00390625, (1024, 1024))
        _af = _a.astype(jnp.float32)
        adj = _af
        return (x, adj)
    x, adj = _rec_inputs()

    def _L0_gnn_setup():
        import jax, jax.numpy as jnp
        import numpy as np
        B, N, D, H = (4, 1024, 256, 8)
        HD = D // H
        key = jax.random.key(seed)
        ks = jax.random.split(key, 10)
        x = jax.random.normal(ks[0], (B, N, D), dtype=jnp.float32)
        adj = (jax.random.uniform(ks[1], (N, N)) < 0.1).astype(jnp.float32)
        s = 1.0 / np.sqrt(D)
        Wq = jax.random.normal(ks[2], (D, D), dtype=jnp.float32) * s
        Wk = jax.random.normal(ks[3], (D, D), dtype=jnp.float32) * s
        Wv = jax.random.normal(ks[4], (D, D), dtype=jnp.float32) * s
        Wo = jax.random.normal(ks[5], (D, D), dtype=jnp.float32) * s
        bq = jnp.zeros((D,), jnp.float32)
        bk = jnp.zeros((D,), jnp.float32)
        bv = jnp.zeros((D,), jnp.float32)
        bo = jnp.zeros((D,), jnp.float32)
        return {'x': x, 'adj': adj, 'Wq': Wq, 'bq': bq, 'Wk': Wk, 'bk': bk, 'Wv': Wv, 'bv': bv, 'Wo': Wo, 'bo': bo}
    _L0_gnn_all = _L0_gnn_setup()
    _L0_gnn_in = {k: v for k, v in _L0_gnn_all.items() if k in ('Wq', 'bq', 'Wk', 'bk', 'Wv', 'bv', 'Wo', 'bo')}
    del _L0_gnn_all
    return {'x': x, 'adj': adj, 'L0_gnn_Wq': _L0_gnn_in['Wq'], 'L0_gnn_bq': _L0_gnn_in['bq'], 'L0_gnn_Wk': _L0_gnn_in['Wk'], 'L0_gnn_bk': _L0_gnn_in['bk'], 'L0_gnn_Wv': _L0_gnn_in['Wv'], 'L0_gnn_bv': _L0_gnn_in['bv'], 'L0_gnn_Wo': _L0_gnn_in['Wo'], 'L0_gnn_bo': _L0_gnn_in['bo']}

def reference(x, adj, L0_gnn_Wq, L0_gnn_bq, L0_gnn_Wk, L0_gnn_bk, L0_gnn_Wv, L0_gnn_bv, L0_gnn_Wo, L0_gnn_bo):
    import jax
    import jax.numpy as jnp

    def _L0_gnn_ref(x, adj, Wq, bq, Wk, bk, Wv, bv, Wo, bo):
        import jax, jax.numpy as jnp
        import numpy as np
        B, N, D, H = (4, 1024, 256, 8)
        HD = D // H
        b, n, d = x.shape
        q = (x @ Wq + bq).reshape(b, n, H, HD)
        k = (x @ Wk + bk).reshape(b, n, H, HD)
        v = (x @ Wv + bv).reshape(b, n, H, HD)
        scores = jnp.einsum('bqhd,bkhd->bhqk', q, k) / jnp.sqrt(jnp.float32(HD))
        scores = scores + (1.0 - adj)[None, None, :, :] * -1000000000.0
        attn = jax.nn.softmax(scores, axis=-1)
        out = jnp.einsum('bhqk,bkhd->bqhd', attn, v).reshape(b, n, d)
        return out @ Wo + bo
    h = jnp.maximum(_layernorm(x, axis=-1), 0.0)
    x = x + _L0_gnn_ref(h, adj, L0_gnn_Wq, L0_gnn_bq, L0_gnn_Wk, L0_gnn_bk, L0_gnn_Wv, L0_gnn_bv, L0_gnn_Wo, L0_gnn_bo)
    return x

_drawn_inputs = setup_inputs


def setup_inputs(seed=0):
    import zlib

    import numpy as np

    out = dict(_drawn_inputs(seed))
    spreads = {'L0_gnn_bq': (0.0, 0.664),
     'L0_gnn_bk': (0.0, 0.8),
     'L0_gnn_bv': (0.0, 0.1),
     'L0_gnn_bo': (0.0, 0.1)}
    factors = {}
    for name, (base, spread) in spreads.items():
        noise = np.random.default_rng([zlib.crc32(name.encode()), seed]).standard_normal(out[name].shape)
        drawn = base * np.exp(spread * noise) if base else spread * noise
        out[name] = jnp.asarray(drawn.astype(out[name].dtype))
    for name, factor in factors.items():
        out[name] = (out[name] * factor).astype(out[name].dtype)
    return out
```

```python
from contextlib import ExitStack

import concourse.bass as bass
from concourse import mybir

F32 = mybir.dt.float32
F32R = mybir.dt.float32r
ALU = mybir.AluOpType
ACT = mybir.ActivationFunctionType

P = 128
DMA = 16


def graph_attention(nc, x, adj, Wq, bq, Wk, bk, Wv, bv, Wo, bo, out):
    B, N, D = x.shape
    HD = 32
    HG = P // HD
    G = D // P
    TILES = N // P
    QH = 512
    HALVES = N // QH
    QT = QH // P
    CHUNKS = G * HALVES
    CU = HG * QT
    U = CHUNKS * CU
    QUARTERS = N // 256
    AHEAD = 3
    RING = AHEAD + 1
    SCALE = -float(HD) ** -0.5
    REP = 4 * HG * DMA

    PREP = [("q", 1, 0, 0), ("k", (1, 0), 4, 0), ("v", (1, 0), 5, 0), ("v", (1, 1), 6, 0), ("k", (1, 1), 8, 0),
            ("q", 2, 14, 0), ("q", 3, 30, 0),
            ("h", 0, 32, 1), ("h", 1, 33, 1), ("h", 2, 40, 1), ("h", 3, 41, 1),
            ("k", (0, 0), 42, 1), ("v", (0, 0), 43, 1), ("v", (0, 1), 44, 1), ("k", (0, 1), 46, 1),
            ("o", (0, 0), 49, 0), ("o", (0, 1), 50, 0), ("q", 0, 52, 1),
            ("o", (1, 0), U, 0), ("o", (1, 1), U, 0)]
    FIRST = [("h", 0), ("h", 1), ("h", 2), ("h", 3), ("k", (0, 0)), ("k", (0, 1)),
             ("v", (0, 0)), ("v", (0, 1)), ("q", 0)]
    STATS_AT = {18: 0, 20: 1, 35: 2, 37: 3}

    NTH = {"h": {q: q + 1 for q in range(QUARTERS)},
           "qk": {("k", (0, 0)): 1, ("k", (0, 1)): 2, ("q", 0): 3, ("q", 1): 4, ("k", (1, 0)): 5, ("k", (1, 1)): 6,
                  ("q", 2): 7, ("q", 3): 8},
           "v": {(0, 0): 1, (0, 1): 2, (1, 0): 3, (1, 1): 4},
           "o": {(0, 0): 1, (0, 1): 2, (1, 0): 3, (1, 1): 4}}
    OPERANDS_FOR_CHUNK = [3, 4, 7, 8]

    def nth(b, what, arg):
        if what in "qk":
            return 8 * b + NTH["qk"][(what, arg)]
        return 4 * b + NTH[what][arg]

    def prep_at(s, last):
        return [(w, a, n) for w, a, at, n in PREP if at == s and not (last and n)]

    def wait_for(eng, semaphore, count, apart=False):
        if isinstance(count, int) and count <= 0:
            return
        eng.wait_ge(semaphore, count)
        if apart:
            eng.sem_inc(wait_passed, 1)

    with ExitStack() as ctx:
        def sb(name, shape, dt=F32):
            return ctx.enter_context(nc.sbuf_tensor(name, shape, dt))

        def ps(name, shape):
            return ctx.enter_context(nc.psum_tensor(name, shape, F32))

        def sem(name):
            return ctx.enter_context(nc.semaphore(name))

        mask = sb("mask", [P, TILES, N])
        k4 = [sb(f"k4_{g}", [P, HG, N], F32R) for g in range(G)]
        q4 = [sb(f"q4_{i}", [P, HG, QH], F32R) for i in range(2)]
        split_hi = sb("split_hi", [P, QH], F32R)
        split_lo = sb("split_lo", [P, QH], F32R)
        v_sb = [sb(f"v_{g}", [P, TILES, P]) for g in range(G)]
        ring = sb("ring", [P, RING, N])
        probs_t = sb("probs_t", [P, HG, TILES, QH])
        xh = sb("xh", [P, 2, 2, D])
        h_t = sb("h_t", [P, G, N])
        attn_t = sb("attn_t", [P, HALVES + 1, QH])
        res = sb("res", [P, 2, 2, D])
        wq_sb, wk_sb, wv_sb, wo_sb = (sb(n, [P, G, D]) for n in ("wq_sb", "wk_sb", "wv_sb", "wo_sb"))
        bq_sb, bk_sb = sb("bq_sb", [P, G]), sb("bk_sb", [P, G])
        bv_sb, bo_sb = sb("bv_sb", [P, D]), sb("bo_sb", [P, D])
        ident = sb("ident", [P, P])
        rowmin, rowsum, rowinv = (sb(n, [P, RING]) for n in ("rowmin", "rowsum", "rowinv"))
        stats = sb("stats", [P, 2, 6])
        moments = sb("moments", [P, 2, 2])
        var_eps, rstd, minus_half = (sb(n, [P, 2]) for n in ("var_eps", "rstd", "minus_half"))

        scores = [ps(f"scores_{i}", [P, N]) for i in range(2)]
        block_t = [ps(f"block_t_{i}", [P, QT * P]) for i in range(2)]
        attn = ps("attn", [P, QH])
        prep = ps("prep", [P, QH])

        adj_loaded = [sem(f"adj_loaded_{i}") for i in range(TILES)]
        wk_loaded, wq_loaded, wv_loaded, wo_loaded = (sem(f"w{n}_loaded") for n in "kqvo")
        biases_loaded = sem("biases_loaded")
        x_loaded = [sem(f"x_loaded_{i}") for i in range(2)]
        res_loaded = [sem(f"res_loaded_{i}") for i in range(2)]
        y_stored = [sem(f"y_stored_{i}") for i in range(2)]
        ident_zeroed, ident_ready = sem("ident_zeroed"), sem("ident_ready")
        half_ready, mask_ready, wq_scaled = sem("half_ready"), sem("mask_ready"), sem("wq_scaled")
        bn_done, aggr_done, var_ready, rstd_ready = (sem(n) for n in ("bn_done", "aggr_done", "var_ready", "rstd_ready"))
        xn_ready = sem("xn_ready")
        product = {"h": sem("h_product"), "qk": sem("qk_product"), "v": sem("v_product"), "o": sem("o_product")}
        h_ready, hi_ready, split_ready, v_ready, y_ready = (
            sem(n) for n in ("h_ready", "hi_ready", "split_ready", "v_ready", "y_ready"))
        spread_done = sem("spread_done")
        res_biased = sem("res_biased")
        scores_ready = sem("scores_ready")
        masked_ready = sem("masked_ready")
        exp_ready = sem("exp_ready")
        inv_ready = sem("inv_ready")
        probs_ready = sem("probs_ready")
        block_ready = [sem(f"block_ready_{i}") for i in range(2)]
        block_taken = [sem(f"block_taken_{i}") for i in range(2)]
        half_used = [sem(f"half_used_{i}") for i in range(2)]
        attn_taken = sem("attn_taken")
        wait_passed = sem("wait_passed")

        def unit(u):
            return u // (HALVES * CU), u // CU % HALVES, u // QT % HG, u % QT

        def quarter_view(t, b, q):
            return t[b, q * 256:(q + 1) * 256, :].rearrange("(t p) d -> p t d", p=P)

        block = ctx.enter_context(nc.Block())

        @block.sync
        def _(sp):
            def spread(b, what, arg):
                wait_for(sp, split_ready, nth(b, what, arg), apart=True)
                back = CU * (arg - 1) if what == "q" else HALVES * CU * (arg[0] - 1)
                wait_for(sp, scores_ready, U * b + back, apart=True)
                for j in range(HG):
                    for r in range(4):
                        if what == "k":
                            part = (split_hi, split_hi, split_lo, split_lo)[r]
                            dst = k4[arg[0]][r * HD:(r + 1) * HD, j, arg[1] * QH:(arg[1] + 1) * QH]
                        else:
                            part = (split_hi, split_lo)[r % 2]
                            dst = q4[arg % 2][r * HD:(r + 1) * HD, j, :]
                        sp.dma_start(dst.bitcast(F32), part[j * HD:(j + 1) * HD, :].bitcast(F32)).then_inc(spread_done, DMA)

            def load_x(b, q):
                sp.dma_start(xh[:, q % 2, :, :], quarter_view(x, b, q)).then_inc(x_loaded[q % 2], DMA)

            def load_res(b, half):
                for p in range(2):
                    wait_for(sp, y_stored[p], DMA * (2 * b + half), apart=True)
                    sp.dma_start(res[:, p, :, :], quarter_view(x, b, 2 * half + p)).then_inc(res_loaded[p], DMA)

            def store_y(b, half):
                for p in range(2):
                    wait_for(sp, y_ready, nth(b, "o", (half, p)), apart=True)
                    sp.dma_start(quarter_view(out, b, 2 * half + p), res[:, p, :, :]).then_inc(y_stored[p], DMA)

            load_x(0, 0)
            load_x(0, 1)
            for v, t in ((bq, bq_sb), (bk, bk_sb)):
                sp.dma_start(t[:, :], v.rearrange("(g p) -> p g", p=P),
                             allow_slow_non_contiguous=True).then_inc(biases_loaded, DMA)
            for v, t in ((bv, bv_sb), (bo, bo_sb)):
                sp.dma_start(t[:, :], v.partition_broadcast(P)).then_inc(biases_loaded, DMA)
            for q in (2, 3):
                wait_for(sp, product["h"], nth(0, "h", q - 2), apart=True)
                load_x(0, q)
            for what, arg in FIRST:
                if what in "qk":
                    spread(0, what, arg)

            def batch(b, last):
                spread(b, "q", 1)
                spread(b, "k", (1, 0))
                spread(b, "k", (1, 1))
                if not last:
                    wait_for(sp, product["h"], nth(b, "h", QUARTERS - 1), apart=True)
                    load_x(b + 1, 0)
                    load_x(b + 1, 1)
                spread(b, "q", 2)
                load_res(b, 0)
                spread(b, "q", 3)
                if not last:
                    for q in (2, 3):
                        wait_for(sp, product["h"], nth(b + 1, "h", q - 2), apart=True)
                        load_x(b + 1, q)
                    spread(b + 1, "k", (0, 0))
                    spread(b + 1, "k", (0, 1))
                store_y(b, 0)
                load_res(b, 1)
                if not last:
                    spread(b + 1, "q", 0)
                store_y(b, 1)

            batch(0, False)
            with sp.Fori(1, B - 1) as b:
                batch(b, False)
            batch(B - 1, True)
            for p in range(2):
                sp.wait_ge(y_stored[p], DMA * 2 * B)

        @block.tensor
        def _(pe):
            def prep_product(b, what, arg):
                if what == "h":
                    wait_for(pe, xn_ready, nth(b, "h", arg))
                    for c in range(G):
                        for t in range(2):
                            mm = pe.transpose(prep[:, (2 * c + t) * P:(2 * c + t + 1) * P],
                                              xh[:, arg % 2, t, c * P:(c + 1) * P], ident[:, :])
                    mm.then_inc(product["h"], 1)
                elif what in "qk":
                    g, half = divmod(arg, HALVES) if what == "q" else arg
                    w = wq_sb if what == "q" else wk_sb
                    for c in range(G):
                        mm = pe.matmul(prep[:, :], w[:, c, g * P:(g + 1) * P], h_t[:, c, half * QH:(half + 1) * QH],
                                       start=(c == 0), stop=(c == G - 1))
                    mm.then_inc(product["qk"], 1)
                elif what == "v":
                    g, half = arg
                    for t in range(QT):
                        at = half * QH + t * P
                        for c in range(G):
                            mm = pe.matmul(prep[:, t * P:(t + 1) * P], h_t[:, c, at:at + P],
                                           wv_sb[:, c, g * P:(g + 1) * P], start=(c == 0), stop=(c == G - 1))
                    mm.then_inc(product["v"], 1)
                else:
                    half, pair = arg
                    wait_for(pe, attn_taken, CHUNKS * b + HALVES + half + 1)
                    for t in range(2):
                        at = (2 * pair + t) * P
                        for g in range(G):
                            mm = pe.matmul(prep[:, t * D:(t + 1) * D], attn_t[:, half if g == 0 else HALVES, at:at + P],
                                           wo_sb[:, g, :], start=(g == 0), stop=(g == G - 1))
                    mm.then_inc(product["o"], 1)

            def prep_bank_free(b, what, arg):
                free = {"h": h_ready, "q": split_ready, "k": split_ready, "v": v_ready, "o": y_ready}[what]
                wait_for(pe, free, nth(b, what, arg))

            def score(b, u):
                g, half, j, qt = unit(u)
                if u % CU == 0:
                    wait_for(pe, spread_done, REP * (8 * b + OPERANDS_FOR_CHUNK[u // CU]))
                wait_for(pe, masked_ready, U * b + u - 1)
                for n in range(N // QH):
                    mm = pe.matmul(scores[u % 2][:, n * QH:(n + 1) * QH], q4[half][:, j, qt * P:(qt + 1) * P],
                                   k4[g][:, j, n * QH:(n + 1) * QH], start=True, stop=True)
                mm.then_inc(scores_ready, 1)

            def transposes(b, u):
                wait_for(pe, probs_ready, U * b + u + 1)
                for i in range(2):
                    wait_for(pe, block_taken[i], U * b + u)
                    for t in range(QT):
                        at = (i * QT + t) * P
                        mm = pe.transpose(block_t[i][:, t * P:(t + 1) * P], ring[:, u % RING, at:at + P], ident[:, :])
                    mm.then_inc(block_ready[i], 1)

            def attend(b, c):
                for i in range(2):
                    wait_for(pe, block_taken[i], U * b + CU * (c + 1))
                wait_for(pe, v_ready, nth(b, "v", (c // HALVES, 1)))
                wait_for(pe, attn_taken, CHUNKS * b + c)
                for kt in range(TILES):
                    for j in range(HG):
                        mm = pe.matmul(attn[j * HD:(j + 1) * HD, :], v_sb[c // HALVES][:, kt, j * HD:(j + 1) * HD],
                                       probs_t[:, j, kt, :], start=(kt == 0), stop=(kt == TILES - 1))
                    if kt % QT == QT - 1:
                        mm.then_inc(half_used[kt // QT], 1)

            pe.wait_ge(ident_ready, 1)
            for n, (what, arg) in enumerate(FIRST):
                if n > 0:
                    prep_bank_free(0, *FIRST[n - 1])
                if (what, arg) == ("k", (0, 0)):
                    pe.wait_ge(wk_loaded, DMA)
                if (what, arg) == ("v", (0, 0)):
                    pe.wait_ge(wv_loaded, DMA)
                if (what, arg) == ("q", 0):
                    pe.wait_ge(wq_scaled, 1)
                prep_product(0, what, arg)
            pe.wait_ge(wo_loaded, DMA)
            for u in range(AHEAD):
                score(0, u)

            def batch(b, last):
                before = None
                for s in range(U):
                    if s + AHEAD < U:
                        score(b, s + AHEAD)
                    elif s < U - 1 and not last:
                        score(b + 1, s + AHEAD - U)
                    for what, arg, n in prep_at(s, last):
                        if before is None:
                            prep_bank_free(b, "q", 0)
                            wait_for(pe, y_ready, 4 * b)
                        else:
                            prep_bank_free(*before)
                        before = (b + n, what, arg)
                        prep_product(*before)
                    if s % CU == 0 and s > 0:
                        attend(b, s // CU - 1)
                    transposes(b, s)
                if not last:
                    score(b + 1, AHEAD - 1)
                attend(b, CHUNKS - 1)
                for what, arg, n in prep_at(U, last):
                    prep_bank_free(*before)
                    before = (b, what, arg)
                    prep_product(*before)

            batch(0, False)
            with pe.Fori(1, B - 1) as b:
                batch(b, False)
            batch(B - 1, True)

        @block.vector
        def _(dve):
            def moments_of(b, q):
                wait_for(dve, x_loaded[q % 2], DMA * (2 * b + q // 2 + 1))
                for t in range(2):
                    bn = dve.bn_stats(stats[:, t, :], xh[:, q % 2, t, :])
                bn.then_inc(bn_done, 1)
                wait_for(dve, bn_done, nth(b, "h", q), apart=True)
                for t in range(2):
                    aggr = dve.bn_aggr(moments[:, t, :], stats[:, t, :])
                aggr.then_inc(aggr_done, 1)
                wait_for(dve, aggr_done, nth(b, "h", q))
                dve.tensor_scalar(var_eps[:, :], moments[:, :, 1], 1e-5, None, ALU.add).then_inc(var_ready, 1)

            def normalise_x(b, q):
                wait_for(dve, rstd_ready, nth(b, "h", q))
                for t in range(2):
                    ts = dve.tensor_scalar(xh[:, q % 2, t, :], xh[:, q % 2, t, :], moments[:, t, 0:1], rstd[:, t:t + 1],
                                           ALU.subtract, ALU.mult)
                ts.then_inc(xn_ready, 1)

            def prep_out(b, what, arg):
                if what in "qk":
                    g = arg // HALVES if what == "q" else arg[0]
                    wait_for(dve, hi_ready, nth(b, what, arg))
                    dve.scalar_tensor_tensor(out=split_lo[:, :], in0=prep[:, :],
                                             scalar=(bq_sb if what == "q" else bk_sb)[:, g:g + 1],
                                             in1=split_hi[:, :].bitcast(F32),
                                             op0=ALU.add, op1=ALU.subtract).then_inc(split_ready, 1)
                elif what == "v":
                    g, half = arg
                    wait_for(dve, product["v"], nth(b, what, arg))
                    wait_for(dve, half_used[1], CHUNKS * b + HALVES * (g - 1))
                    bias = bv_sb[:, g * P:(g + 1) * P].unsqueeze(1).broadcast_to([P, QT, P])
                    dve.tensor_tensor(v_sb[g][:, half * QT:(half + 1) * QT, :],
                                      prep[:, :].rearrange("p (t n) -> p t n", n=P), bias, ALU.add).then_inc(v_ready, 1)
                elif what == "o":
                    half, pair = arg
                    wait_for(dve, product["o"], nth(b, what, arg))
                    wait_for(dve, res_biased, nth(b, what, arg))
                    dve.tensor_tensor(res[:, pair, :, :], prep[:, :].rearrange("p (t n) -> p t n", n=D),
                                      res[:, pair, :, :], ALU.add).then_inc(y_ready, 1)

            def mask_and_min(b, u):
                g, half, j, qt = unit(u)
                dve.wait_ge(mask_ready, half * QT + qt + 1)
                wait_for(dve, block_ready[1], U * b + u + 1 - RING)
                wait_for(dve, scores_ready, U * b + u + 1, apart=True)
                slot = u % RING
                dve.tensor_tensor_reduce(ring[:, slot, :], scores[u % 2][:, :], mask[:, half * QT + qt, :], 1.0, 3.4e38,
                                         ALU.add, ALU.min, rowmin[:, slot:slot + 1]).then_inc(masked_ready, 1)

            def invert_sum(b, u):
                wait_for(dve, exp_ready, U * b + u + 1)
                slot = u % RING
                dve.reciprocal(rowinv[:, slot:slot + 1], rowsum[:, slot:slot + 1]).then_inc(inv_ready, 1)

            def take_block(b, u):
                g, half, j, qt = unit(u)
                wait_for(dve, block_ready[0], U * b + u + 1)
                if u % CU == 0:
                    wait_for(dve, half_used[0], CHUNKS * b + u // CU)
                dve.tensor_copy(probs_t[:, j, 0:QT, qt * P:(qt + 1) * P],
                                block_t[0][:, :].rearrange("p (t n) -> p t n", n=P)).then_inc(block_taken[0], 1)

            for q in range(QUARTERS):
                moments_of(0, q)
                normalise_x(0, q)
            dve.wait_ge(wq_loaded, DMA)
            dve.wait_ge(biases_loaded, 4 * DMA)
            dve.tensor_scalar(bq_sb[:, :], bq_sb[:, :], SCALE, None, ALU.mult)
            dve.tensor_scalar(wq_sb[:, :, :], wq_sb[:, :, :], SCALE, None, ALU.mult).then_inc(wq_scaled, 1)
            dve.wait_ge(wq_scaled, 1)
            for what, arg in FIRST:
                prep_out(0, what, arg)
            for u in range(AHEAD):
                mask_and_min(0, u)
            for u in range(AHEAD - 1):
                invert_sum(0, u)

            def batch(b, last):
                for s in range(U):
                    if s == U - 1:
                        take_block(b, s)
                    if s + AHEAD < U:
                        mask_and_min(b, s + AHEAD)
                    elif not last:
                        mask_and_min(b + 1, s + AHEAD - U)
                    if s < U - 1:
                        take_block(b, s)
                    if s + AHEAD - 1 < U:
                        invert_sum(b, s + AHEAD - 1)
                    elif not last:
                        invert_sum(b + 1, s + AHEAD - 1 - U)
                    for what, arg, n in prep_at(s, last):
                        prep_out(b + n, what, arg)
                    if not last:
                        if s in STATS_AT:
                            moments_of(b + 1, STATS_AT[s])
                        if s - 1 in STATS_AT:
                            normalise_x(b + 1, STATS_AT[s - 1])
                for what, arg, n in prep_at(U, last):
                    prep_out(b, what, arg)

            batch(0, False)
            with dve.Fori(1, B - 1) as b:
                batch(b, False)
            batch(B - 1, True)

        @block.scalar
        def _(act):
            def prep_out(b, what, arg):
                if what == "h":
                    wait_for(act, product["h"], nth(b, what, arg))
                    act.activation(h_t[:, :, arg * 256:(arg + 1) * 256], prep[:, :].rearrange("p (c n) -> p c n", c=G),
                                   ACT.Relu).then_inc(h_ready, 1)
                elif what in "qk":
                    g = arg // HALVES if what == "q" else arg[0]
                    wait_for(act, product["qk"], nth(b, what, arg))
                    wait_for(act, spread_done, REP * (nth(b, what, arg) - 1))
                    act.activation(split_hi[:, :], prep[:, :], ACT.Identity,
                                   bias=(bq_sb if what == "q" else bk_sb)[:, g:g + 1]).then_inc(hi_ready, 1)

            def exponential(b, u):
                wait_for(act, masked_ready, U * b + u + 1)
                slot = u % RING
                act.activation(ring[:, slot, :], ring[:, slot, :], ACT.Exp, bias=rowmin[:, slot:slot + 1], scale=-1.0,
                               accum_out=rowsum[:, slot:slot + 1]).then_inc(exp_ready, 1)

            def take_block(b, u):
                g, half, j, qt = unit(u)
                wait_for(act, block_ready[1], U * b + u + 1)
                if u % CU == 0:
                    wait_for(act, half_used[1], CHUNKS * b + u // CU)
                act.copy(probs_t[:, j, QT:TILES, qt * P:(qt + 1) * P],
                         block_t[1][:, :].rearrange("p (t n) -> p t n", n=P)).then_inc(block_taken[1], 1)

            def take_attn(b, c):
                wait_for(act, half_used[1], CHUNKS * b + c + 1)
                act.copy(attn_t[:, min(c, HALVES), :], attn[:, :]).then_inc(attn_taken, 1)

            for i in range(TILES):
                act.dma_start(mask[:, i, :], adj[i * P:(i + 1) * P, :]).then_inc(adj_loaded[i], DMA)
            for n, (what, arg) in enumerate(FIRST):
                if n == QUARTERS:
                    act.wait_ge(biases_loaded, 4 * DMA)
                    act.wait_ge(wq_scaled, 1)
                prep_out(0, what, arg)
            for u in range(AHEAD):
                exponential(0, u)

            def batch(b, last):
                for s in range(U):
                    busy = s % CU == 0 or prep_at(s, last)
                    if not busy:
                        take_block(b, s)
                    if s + AHEAD < U:
                        exponential(b, s + AHEAD)
                    elif not last:
                        exponential(b + 1, s + AHEAD - U)
                    for what, arg, n in prep_at(s, last):
                        prep_out(b + n, what, arg)
                    if s % CU == 0 and s > 0:
                        take_attn(b, s // CU - 1)
                    if busy:
                        take_block(b, s)
                take_attn(b, CHUNKS - 1)

            batch(0, False)
            with act.Fori(1, B - 1) as b:
                batch(b, False)
            batch(B - 1, True)

        @block.gpsimd
        def _(pool):
            def root(b, q):
                wait_for(pool, var_ready, nth(b, "h", q))
                pool.tensor_tensor(rstd[:, :], var_eps[:, :], minus_half[:, :], ALU.pow).then_inc(rstd_ready, 1)

            def divide(b, u):
                wait_for(pool, inv_ready, U * b + u + 1, apart=True)
                slot = u % RING
                pool.tensor_scalar(ring[:, slot, :], ring[:, slot, :], rowinv[:, slot:slot + 1], 1.0,
                                   ALU.mult, ALU.mult).then_inc(probs_ready, 1)

            def bias_res(b, half):
                for p in range(2):
                    wait_for(pool, res_loaded[p], DMA * (2 * b + half + 1))
                    bias = bo_sb[:, :].unsqueeze(1).broadcast_to([P, 2, D])
                    pool.tensor_tensor(res[:, p, :, :], res[:, p, :, :], bias, ALU.add).then_inc(res_biased, 1)

            for w, t, loaded in ((Wk, wk_sb, wk_loaded), (Wq, wq_sb, wq_loaded), (Wv, wv_sb, wv_loaded),
                                 (Wo, wo_sb, wo_loaded)):
                pool.dma_start(t[:, :, :], w.rearrange("(c p) n -> p c n", p=P)).then_inc(loaded, DMA)
            pool.memset(minus_half[:, :], -0.5).then_inc(half_ready, 1)
            pool.memset(ident[:, :], 0.0).then_inc(ident_zeroed, 1)
            pool.wait_ge(ident_zeroed, 1)
            pool.affine_select(out=ident[:, :], in_=ident[:, :], compare_op=ALU.not_equal, fill=1.0, base=0,
                               pattern=[[-1, P]], channel_multiplier=1).then_inc(ident_ready, 1)
            pool.wait_ge(half_ready, 1)
            for q in range(QUARTERS):
                root(0, q)
            for i in range(TILES):
                pool.wait_ge(adj_loaded[i], DMA)
                pool.tensor_scalar(mask[:, i, :], mask[:, i, :], -1.0, -1e9, ALU.add, ALU.mult).then_inc(mask_ready, 1)
            pool.wait_ge(biases_loaded, 4 * DMA)

            def batch(b, last):
                for u in range(U):
                    divide(b, u)
                    at = u - AHEAD + 1
                    if at in STATS_AT and not last:
                        root(b + 1, STATS_AT[at])
                    if u in (3 * CU - 6, U - 6):
                        bias_res(b, u // (3 * CU))

            batch(0, False)
            with pool.Fori(1, B - 1) as b:
                batch(b, False)
            batch(B - 1, True)


_INS = ["x", "adj", "L0_gnn_Wq", "L0_gnn_bq", "L0_gnn_Wk", "L0_gnn_bk", "L0_gnn_Wv", "L0_gnn_bv", "L0_gnn_Wo", "L0_gnn_bo"]


def kernel(**inputs):
    import numpy as _np
    import concourse.bacc as _bacc
    from concourse import mybir as _mybir
    from concourse.bass_utils import run_bass_kernel_spmd as _run

    nc = _bacc.Bacc("TRN2", target_bir_lowering=False, num_devices=1)
    arrays, args = {}, []
    for name in _INS:
        a = _np.ascontiguousarray(inputs[name])
        arrays[f"in_{name}_dram"] = a
        args.append(nc.dram_tensor(f"in_{name}_dram", a.shape, _mybir.dt.from_np(a.dtype), kind="ExternalInput").ap())
    shape = arrays["in_x_dram"].shape
    args.append(nc.dram_tensor("out_0_dram", shape, _mybir.dt.float32, kind="ExternalOutput").ap())
    graph_attention(nc, *args)
    r = _run(nc, [arrays], core_ids=[0])
    return r.results[0]["out_0_dram"]
```

```python
from contextlib import ExitStack

import concourse.bass as bass
from concourse import mybir

F32 = mybir.dt.float32
F32R = mybir.dt.float32r
ALU = mybir.AluOpType
ACT = mybir.ActivationFunctionType

P = 128
DMA = 16


def graph_attention(nc, x, adj, Wq, bq, Wk, bk, Wv, bv, Wo, bo, out):
    B, N, D = x.shape
    HD = 32
    HG = P // HD
    G = D // P
    TILES = N // P
    QH = 512
    HALVES = N // QH
    QT = QH // P
    CHUNKS = G * HALVES
    CU = HG * QT
    U = CHUNKS * CU
    QUARTERS = N // 256
    AHEAD = 5
    RING = 8
    HEADS = U // QT
    SCALE = -float(HD) ** -0.5
    REP = 2 * HG * DMA

    PREP = [("q", 1, 0, 0), ("s", 3, 4, -1), ("o", (1, 0), 6, -1), ("o", (1, 1), 8, -1),
            ("v", (1, 0), 9, 0), ("k", (1, 0), 10, 0), ("v", (1, 1), 12, 0), ("k", (1, 1), 14, 0),
            ("q", 2, 18, 0), ("s", 0, 20, 0), ("q", 3, 31, 0),
            ("h", 0, 33, 1), ("h", 1, 34, 1), ("s", 1, 36, 0), ("h", 2, 41, 1), ("h", 3, 42, 1),
            ("k", (0, 0), 44, 1), ("v", (0, 0), 45, 1), ("v", (0, 1), 46, 1), ("k", (0, 1), 48, 1),
            ("q", 0, 52, 1), ("s", 2, 53, 0), ("o", (0, 0), 55, 0), ("o", (0, 1), 57, 0)]
    FIRST = [("h", 0), ("h", 1), ("h", 2), ("h", 3), ("k", (0, 0)), ("k", (0, 1)),
             ("v", (0, 0)), ("v", (0, 1)), ("q", 0)]
    STATS_AT = {22: 0, 24: 1, 36: 2, 38: 3}

    NTH = {"h": {q: q + 1 for q in range(QUARTERS)},
           "qk": {("k", (0, 0)): 1, ("k", (0, 1)): 2, ("q", 0): 3, ("q", 1): 4, ("k", (1, 0)): 5, ("k", (1, 1)): 6,
                  ("q", 2): 7, ("q", 3): 8},
           "s": {c: c + 1 for c in range(CHUNKS)},
           "v": {(0, 0): 1, (0, 1): 2, (1, 0): 3, (1, 1): 4},
           "o": {(0, 0): 1, (0, 1): 2, (1, 0): 3, (1, 1): 4}}
    OPERANDS_FOR_CHUNK = [3, 4, 7, 8]

    def nth(b, what, arg):
        if what in "qk":
            return 8 * b + NTH["qk"][(what, arg)]
        return 4 * b + NTH[what][arg]

    def prep_at(s, first, last):
        return [(w, a, n) for w, a, at, n in PREP if at == s and not (first and n < 0 or last and n > 0)]

    AFTER = [(w, a) for w, a, _, n in PREP if n < 0]

    def wait_for(eng, semaphore, count, apart=False):
        if isinstance(count, int) and count <= 0:
            return
        eng.wait_ge(semaphore, count)
        if apart:
            eng.sem_inc(wait_passed, 1)

    with ExitStack() as ctx:
        def sb(name, shape, dt=F32):
            return ctx.enter_context(nc.sbuf_tensor(name, shape, dt))

        def ps(name, shape):
            return ctx.enter_context(nc.psum_tensor(name, shape, F32))

        def sem(name):
            return ctx.enter_context(nc.semaphore(name))

        mask = sb("mask", [P, TILES, N])
        k4 = [sb(f"k4_{g}", [P, HG, N], F32R) for g in range(G)]
        q4 = [sb(f"q4_{i}", [P, HG, QH], F32R) for i in range(2)]
        split = sb("split", [P, 2, QH], F32R)
        v_sb = [sb(f"v_{g}", [P, TILES, P]) for g in range(G)]
        ring = sb("ring", [P, RING, N])
        probs_t = sb("probs_t", [P, 2, TILES, QH])
        parts_sb = sb("parts_sb", [P, HG, QH])
        adder = sb("adder", [P, HD])
        xh = sb("xh", [P, 2, 2, D])
        h_t = sb("h_t", [P, G, N])
        attn_t = sb("attn_t", [P, HALVES + 1, QH])
        res = sb("res", [P, 2, 2, D])
        wq_sb, wk_sb, wv_sb, wo_sb = (sb(n, [P, G, D]) for n in ("wq_sb", "wk_sb", "wv_sb", "wo_sb"))
        bq_sb, bk_sb = sb("bq_sb", [P, G]), sb("bk_sb", [P, G])
        bv_sb, bo_sb = sb("bv_sb", [P, D]), sb("bo_sb", [P, D])
        ident = sb("ident", [P, P])
        rowmin, rowsum, rowinv = (sb(n, [P, RING]) for n in ("rowmin", "rowsum", "rowinv"))
        stats = sb("stats", [P, 2, 6])
        moments = sb("moments", [P, 2, 2])
        var_eps, rstd, minus_half = (sb(n, [P, 2]) for n in ("var_eps", "rstd", "minus_half"))

        scores = [ps(f"scores_{i}", [P, N]) for i in range(2)]
        block_t = [ps(f"block_t_{i}", [P, QT * P]) for i in range(2)]
        parts = ps("parts", [P, QH])
        prep = ps("prep", [P, QH])

        adj_loaded = [sem(f"adj_loaded_{i}") for i in range(TILES)]
        wk_loaded, wq_loaded, wv_loaded, wo_loaded = (sem(f"w{n}_loaded") for n in "kqvo")
        biases_loaded = sem("biases_loaded")
        x_loaded = [sem(f"x_loaded_{i}") for i in range(2)]
        res_loaded = [sem(f"res_loaded_{i}") for i in range(2)]
        y_stored = [sem(f"y_stored_{i}") for i in range(2)]
        ident_zeroed, ident_ready = sem("ident_zeroed"), sem("ident_ready")
        adder_ready = sem("adder_ready")
        half_ready, mask_ready, wq_scaled = sem("half_ready"), sem("mask_ready"), sem("wq_scaled")
        bn_done, aggr_done, var_ready, rstd_ready = (sem(n) for n in ("bn_done", "aggr_done", "var_ready", "rstd_ready"))
        xn_ready = sem("xn_ready")
        product = {"h": sem("h_product"), "qk": sem("qk_product"), "v": sem("v_product"), "o": sem("o_product"),
                   "s": sem("s_product")}
        h_ready, hi_ready, split_ready, v_ready, y_ready = (
            sem(n) for n in ("h_ready", "hi_ready", "split_ready", "v_ready", "y_ready"))
        spread_done = sem("spread_done")
        res_biased = sem("res_biased")
        scores_ready = sem("scores_ready")
        masked_ready = sem("masked_ready")
        exp_ready = sem("exp_ready")
        inv_ready = sem("inv_ready")
        probs_ready = sem("probs_ready")
        block_ready = [sem(f"block_ready_{i}") for i in range(2)]
        block_taken = [sem(f"block_taken_{i}") for i in range(2)]
        half_used = [sem(f"half_used_{i}") for i in range(2)]
        parts_taken = sem("parts_taken")
        attn_ready = sem("attn_ready")
        wait_passed = sem("wait_passed")

        def unit(u):
            return u // (HALVES * CU), u // CU % HALVES, u // QT % HG, u % QT

        def quarter_view(t, b, q):
            return t[b, q * 256:(q + 1) * 256, :].rearrange("(t p) d -> p t d", p=P)

        block = ctx.enter_context(nc.Block())

        @block.sync
        def _(sp):
            def spread(b, what, arg):
                wait_for(sp, split_ready, nth(b, what, arg), apart=True)
                back = CU * (arg - 1) if what == "q" else HALVES * CU * (arg[0] - 1)
                wait_for(sp, scores_ready, U * b + back, apart=True)
                for j in range(HG):
                    rows = split[j * HD:(j + 1) * HD, :, :].bitcast(F32)
                    for r in range(2):
                        if what == "k":
                            dst = k4[arg[0]][r * 2 * HD:(r + 1) * 2 * HD, j, arg[1] * QH:(arg[1] + 1) * QH]
                            src = rows[:, r, :].unsqueeze(1).broadcast_to([HD, 2, QH])
                        else:
                            dst = q4[arg % 2][r * 2 * HD:(r + 1) * 2 * HD, j, :]
                            src = rows
                        sp.dma_start(dst.bitcast(F32), src).then_inc(spread_done, DMA)

            def load_x(b, q):
                sp.dma_start(xh[:, q % 2, :, :], quarter_view(x, b, q)).then_inc(x_loaded[q % 2], DMA)

            def load_res(b, half):
                for p in range(2):
                    wait_for(sp, y_stored[p], DMA * (2 * b + half), apart=True)
                    sp.dma_start(res[:, p, :, :], quarter_view(x, b, 2 * half + p)).then_inc(res_loaded[p], DMA)

            def store_y(b, half):
                for p in range(2):
                    wait_for(sp, y_ready, nth(b, "o", (half, p)), apart=True)
                    sp.dma_start(quarter_view(out, b, 2 * half + p), res[:, p, :, :]).then_inc(y_stored[p], DMA)

            load_x(0, 0)
            load_x(0, 1)
            for v, t in ((bq, bq_sb), (bk, bk_sb)):
                sp.dma_start(t[:, :], v.rearrange("(g p) -> p g", p=P),
                             allow_slow_non_contiguous=True).then_inc(biases_loaded, DMA)
            for v, t in ((bv, bv_sb), (bo, bo_sb)):
                sp.dma_start(t[:, :], v.partition_broadcast(P)).then_inc(biases_loaded, DMA)
            for q in (2, 3):
                wait_for(sp, product["h"], nth(0, "h", q - 2), apart=True)
                load_x(0, q)
            for what, arg in FIRST:
                if what in "qk":
                    spread(0, what, arg)

            def batch(b, first=False, last=False):
                spread(b, "q", 1)
                if not first:
                    store_y(b - 1, 1)
                load_res(b, 0)
                spread(b, "k", (1, 0))
                spread(b, "k", (1, 1))
                if not last:
                    wait_for(sp, product["h"], nth(b, "h", QUARTERS - 1), apart=True)
                    load_x(b + 1, 0)
                    load_x(b + 1, 1)
                spread(b, "q", 2)
                spread(b, "q", 3)
                if not last:
                    for q in (2, 3):
                        wait_for(sp, product["h"], nth(b + 1, "h", q - 2), apart=True)
                        load_x(b + 1, q)
                    spread(b + 1, "k", (0, 0))
                    spread(b + 1, "k", (0, 1))
                    spread(b + 1, "q", 0)
                store_y(b, 0)
                load_res(b, 1)

            batch(0, first=True)
            with sp.Fori(1, B - 1) as b:
                batch(b)
            batch(B - 1, last=True)
            store_y(B - 1, 1)
            for p in range(2):
                sp.wait_ge(y_stored[p], DMA * 2 * B)

        @block.tensor
        def _(pe):
            def prep_product(b, what, arg):
                if what == "h":
                    wait_for(pe, xn_ready, nth(b, "h", arg))
                    for c in range(G):
                        for t in range(2):
                            mm = pe.transpose(prep[:, (2 * c + t) * P:(2 * c + t + 1) * P],
                                              xh[:, arg % 2, t, c * P:(c + 1) * P], ident[:, :])
                    mm.then_inc(product["h"], 1)
                elif what in "qk":
                    g, half = divmod(arg, HALVES) if what == "q" else arg
                    w = wq_sb if what == "q" else wk_sb
                    for c in range(G):
                        mm = pe.matmul(prep[:, :], w[:, c, g * P:(g + 1) * P], h_t[:, c, half * QH:(half + 1) * QH],
                                       start=(c == 0), stop=(c == G - 1))
                    mm.then_inc(product["qk"], 1)
                elif what == "v":
                    g, half = arg
                    for t in range(QT):
                        at = half * QH + t * P
                        for c in range(G):
                            mm = pe.matmul(prep[:, t * P:(t + 1) * P], h_t[:, c, at:at + P],
                                           wv_sb[:, c, g * P:(g + 1) * P], start=(c == 0), stop=(c == G - 1))
                    mm.then_inc(product["v"], 1)
                elif what == "s":
                    wait_for(pe, parts_taken, HEADS * b + HG * (arg + 1))
                    for j in range(HG):
                        mm = pe.matmul(prep[j * HD:(j + 1) * HD, :], adder[:, :], parts_sb[:, j, :], start=True, stop=True)
                    mm.then_inc(product["s"], 1)
                else:
                    half, pair = arg
                    wait_for(pe, attn_ready, nth(b, "s", HALVES + half))
                    for t in range(2):
                        at = (2 * pair + t) * P
                        for g in range(G):
                            mm = pe.matmul(prep[:, t * D:(t + 1) * D], attn_t[:, half if g == 0 else HALVES, at:at + P],
                                           wo_sb[:, g, :], start=(g == 0), stop=(g == G - 1))
                    mm.then_inc(product["o"], 1)

            def prep_bank_free(b, what, arg):
                free = {"h": h_ready, "q": split_ready, "k": split_ready, "v": v_ready, "o": y_ready,
                        "s": attn_ready}[what]
                wait_for(pe, free, nth(b, what, arg))

            def score(b, u):
                g, half, j, qt = unit(u)
                if u % CU == 0:
                    wait_for(pe, spread_done, REP * (8 * b + OPERANDS_FOR_CHUNK[u // CU]))
                wait_for(pe, masked_ready, U * b + u - 1)
                for n in range(N // QH):
                    mm = pe.matmul(scores[u % 2][:, n * QH:(n + 1) * QH], q4[half][:, j, qt * P:(qt + 1) * P],
                                   k4[g][:, j, n * QH:(n + 1) * QH], start=True, stop=True)
                mm.then_inc(scores_ready, 1)

            def transposes(b, u):
                wait_for(pe, probs_ready, U * b + u + 1)
                for i in range(2):
                    wait_for(pe, block_taken[i], U * b + u)
                    for t in range(QT):
                        at = (i * QT + t) * P
                        mm = pe.transpose(block_t[i][:, t * P:(t + 1) * P], ring[:, u % RING, at:at + P], ident[:, :])
                    mm.then_inc(block_ready[i], 1)

            def attend(b, n, i):
                g, half, j, _ = unit(QT * n)
                wait_for(pe, block_taken[i], U * b + QT * (n + 1))
                if i == 0:
                    wait_for(pe, v_ready, nth(b, "v", (g, 1)))
                    wait_for(pe, parts_taken, HEADS * b + n)
                for t in range(QT):
                    mm = pe.matmul(parts[t * HD:(t + 1) * HD, :], v_sb[g][:, i * QT + t, j * HD:(j + 1) * HD],
                                   probs_t[:, j % 2, i * QT + t, :], start=(i == 0), stop=(i == 1))
                mm.then_inc(half_used[i], 1)

            pe.wait_ge(ident_ready, 1)
            for n, (what, arg) in enumerate(FIRST):
                if n > 0:
                    prep_bank_free(0, *FIRST[n - 1])
                if (what, arg) == ("k", (0, 0)):
                    pe.wait_ge(wk_loaded, DMA)
                if (what, arg) == ("v", (0, 0)):
                    pe.wait_ge(wv_loaded, DMA)
                if (what, arg) == ("q", 0):
                    pe.wait_ge(wq_scaled, 1)
                prep_product(0, what, arg)
            pe.wait_ge(wo_loaded, DMA)
            pe.wait_ge(adder_ready, 1)
            for u in range(AHEAD):
                score(0, u)

            def prep_next(before, b, what, arg):
                prep_bank_free(*before)
                prep_product(b, what, arg)
                return b, what, arg

            def batch(b, first=False, last=False):
                before = (0, *FIRST[-1]) if first else (b - 1, "o", (0, 1))
                for s in range(U):
                    if s + AHEAD < U:
                        score(b, s + AHEAD)
                    elif not last:
                        score(b + 1, s + AHEAD - U)
                    for what, arg, n in prep_at(s, first, last):
                        before = prep_next(before, b + n, what, arg)
                    if s % QT in (1, 2):
                        if s > QT:
                            attend(b, s // QT - 1, s % QT - 1)
                        elif not first:
                            attend(b - 1, HEADS - 1, s % QT - 1)
                    transposes(b, s)

            batch(0, first=True)
            with pe.Fori(1, B - 1) as b:
                batch(b)
            batch(B - 1, last=True)
            attend(B - 1, HEADS - 1, 0)
            attend(B - 1, HEADS - 1, 1)
            before = (B - 1, "o", (0, 1))
            for what, arg in AFTER:
                before = prep_next(before, B - 1, what, arg)

        @block.vector
        def _(dve):
            def moments_of(b, q):
                wait_for(dve, x_loaded[q % 2], DMA * (2 * b + q // 2 + 1))
                for t in range(2):
                    bn = dve.bn_stats(stats[:, t, :], xh[:, q % 2, t, :])
                bn.then_inc(bn_done, 1)
                wait_for(dve, bn_done, nth(b, "h", q), apart=True)
                for t in range(2):
                    aggr = dve.bn_aggr(moments[:, t, :], stats[:, t, :])
                aggr.then_inc(aggr_done, 1)
                wait_for(dve, aggr_done, nth(b, "h", q))
                dve.tensor_scalar(var_eps[:, :], moments[:, :, 1], 1e-5, None, ALU.add).then_inc(var_ready, 1)

            def normalise_x(b, q):
                wait_for(dve, rstd_ready, nth(b, "h", q))
                for t in range(2):
                    ts = dve.tensor_scalar(xh[:, q % 2, t, :], xh[:, q % 2, t, :], moments[:, t, 0:1], rstd[:, t:t + 1],
                                           ALU.subtract, ALU.mult)
                ts.then_inc(xn_ready, 1)

            def prep_out(b, what, arg):
                if what in "qk":
                    g = arg // HALVES if what == "q" else arg[0]
                    wait_for(dve, hi_ready, nth(b, what, arg))
                    dve.scalar_tensor_tensor(out=split[:, 1, :], in0=prep[:, :],
                                             scalar=(bq_sb if what == "q" else bk_sb)[:, g:g + 1],
                                             in1=split[:, 0, :].bitcast(F32),
                                             op0=ALU.add, op1=ALU.subtract).then_inc(split_ready, 1)
                elif what == "v":
                    g, half = arg
                    wait_for(dve, product["v"], nth(b, what, arg))
                    wait_for(dve, half_used[1], HEADS * b + HEADS // G * (g - 1))
                    bias = bv_sb[:, g * P:(g + 1) * P].unsqueeze(1).broadcast_to([P, QT, P])
                    dve.tensor_tensor(v_sb[g][:, half * QT:(half + 1) * QT, :],
                                      prep[:, :].rearrange("p (t n) -> p t n", n=P), bias, ALU.add).then_inc(v_ready, 1)
                elif what == "o":
                    half, pair = arg
                    wait_for(dve, product["o"], nth(b, what, arg))
                    wait_for(dve, res_biased, nth(b, what, arg))
                    dve.tensor_tensor(res[:, pair, :, :], prep[:, :].rearrange("p (t n) -> p t n", n=D),
                                      res[:, pair, :, :], ALU.add).then_inc(y_ready, 1)

            def mask_and_min(b, u):
                g, half, j, qt = unit(u)
                dve.wait_ge(mask_ready, half * QT + qt + 1)
                wait_for(dve, block_ready[1], U * b + u + 1 - RING)
                wait_for(dve, scores_ready, U * b + u + 1, apart=True)
                slot = u % RING
                dve.tensor_tensor_reduce(ring[:, slot, :], scores[u % 2][:, :], mask[:, half * QT + qt, :], 1.0, 3.4e38,
                                         ALU.add, ALU.min, rowmin[:, slot:slot + 1]).then_inc(masked_ready, 1)

            def invert_sum(b, u):
                wait_for(dve, exp_ready, U * b + u + 1)
                slot = u % RING
                dve.reciprocal(rowinv[:, slot:slot + 1], rowsum[:, slot:slot + 1]).then_inc(inv_ready, 1)

            def take_block(b, u):
                g, half, j, qt = unit(u)
                wait_for(dve, block_ready[0], U * b + u + 1)
                if u % QT == 0:
                    wait_for(dve, half_used[0], HEADS * b + u // QT - 1)
                dve.tensor_copy(probs_t[:, j % 2, 0:QT, qt * P:(qt + 1) * P],
                                block_t[0][:, :].rearrange("p (t n) -> p t n", n=P)).then_inc(block_taken[0], 1)

            for q in range(QUARTERS):
                moments_of(0, q)
                normalise_x(0, q)
            dve.wait_ge(wq_loaded, DMA)
            dve.wait_ge(biases_loaded, 4 * DMA)
            dve.tensor_scalar(bq_sb[:, :], bq_sb[:, :], SCALE, None, ALU.mult)
            dve.tensor_scalar(wq_sb[:, :, :], wq_sb[:, :, :], SCALE, None, ALU.mult).then_inc(wq_scaled, 1)
            dve.wait_ge(wq_scaled, 1)
            for what, arg in FIRST:
                prep_out(0, what, arg)
            for u in range(AHEAD):
                mask_and_min(0, u)
            for u in range(AHEAD - 1):
                invert_sum(0, u)

            def batch(b, first=False, last=False):
                for s in range(U):
                    if s + AHEAD < U:
                        mask_and_min(b, s + AHEAD)
                    elif not last:
                        mask_and_min(b + 1, s + AHEAD - U)
                    take_block(b, s)
                    if s + AHEAD - 1 < U:
                        invert_sum(b, s + AHEAD - 1)
                    elif not last:
                        invert_sum(b + 1, s + AHEAD - 1 - U)
                    for what, arg, n in prep_at(s, first, last):
                        prep_out(b + n, what, arg)
                    if not last:
                        if s in STATS_AT:
                            moments_of(b + 1, STATS_AT[s])
                        if s - 1 in STATS_AT:
                            normalise_x(b + 1, STATS_AT[s - 1])

            batch(0, first=True)
            with dve.Fori(1, B - 1) as b:
                batch(b)
            batch(B - 1, last=True)
            for what, arg in AFTER:
                prep_out(B - 1, what, arg)

        @block.scalar
        def _(act):
            def prep_out(b, what, arg):
                if what == "h":
                    wait_for(act, product["h"], nth(b, what, arg))
                    act.activation(h_t[:, :, arg * 256:(arg + 1) * 256], prep[:, :].rearrange("p (c n) -> p c n", c=G),
                                   ACT.Relu).then_inc(h_ready, 1)
                elif what in "qk":
                    g = arg // HALVES if what == "q" else arg[0]
                    wait_for(act, product["qk"], nth(b, what, arg))
                    wait_for(act, spread_done, REP * (nth(b, what, arg) - 1))
                    act.activation(split[:, 0, :], prep[:, :], ACT.Identity,
                                   bias=(bq_sb if what == "q" else bk_sb)[:, g:g + 1]).then_inc(hi_ready, 1)
                elif what == "s":
                    wait_for(act, product["s"], nth(b, what, arg))
                    act.copy(attn_t[:, min(arg, HALVES), :], prep[:, :]).then_inc(attn_ready, 1)

            def exponential(b, u):
                wait_for(act, masked_ready, U * b + u + 1)
                slot = u % RING
                act.activation(ring[:, slot, :], ring[:, slot, :], ACT.Exp, bias=rowmin[:, slot:slot + 1], scale=-1.0,
                               accum_out=rowsum[:, slot:slot + 1]).then_inc(exp_ready, 1)

            def take_block(b, u):
                g, half, j, qt = unit(u)
                wait_for(act, block_ready[1], U * b + u + 1)
                if u % QT == 0:
                    wait_for(act, half_used[1], HEADS * b + u // QT - 1)
                act.copy(probs_t[:, j % 2, QT:TILES, qt * P:(qt + 1) * P],
                         block_t[1][:, :].rearrange("p (t n) -> p t n", n=P)).then_inc(block_taken[1], 1)

            def take_parts(b, n):
                wait_for(act, half_used[1], HEADS * b + n + 1)
                if n % HG == 0:
                    wait_for(act, product["s"], CHUNKS * b + n // HG)
                act.copy(parts_sb[:, n % HG, :], parts[:, :]).then_inc(parts_taken, 1)

            for i in range(TILES):
                act.dma_start(mask[:, i, :], adj[i * P:(i + 1) * P, :]).then_inc(adj_loaded[i], DMA)
            for n, (what, arg) in enumerate(FIRST):
                if n == QUARTERS:
                    act.wait_ge(biases_loaded, 4 * DMA)
                    act.wait_ge(wq_scaled, 1)
                prep_out(0, what, arg)
            for u in range(AHEAD):
                exponential(0, u)

            def batch(b, first=False, last=False):
                for s in range(U):
                    busy = prep_at(s, first, last)
                    if not busy:
                        take_block(b, s)
                    if s + AHEAD < U:
                        exponential(b, s + AHEAD)
                    elif not last:
                        exponential(b + 1, s + AHEAD - U)
                    for what, arg, n in busy:
                        prep_out(b + n, what, arg)
                    if busy:
                        take_block(b, s)
                    if s % QT == 2:
                        if s > QT:
                            take_parts(b, s // QT - 1)
                        elif not first:
                            take_parts(b - 1, HEADS - 1)

            batch(0, first=True)
            with act.Fori(1, B - 1) as b:
                batch(b)
            batch(B - 1, last=True)
            take_parts(B - 1, HEADS - 1)
            for what, arg in AFTER:
                prep_out(B - 1, what, arg)

        @block.gpsimd
        def _(pool):
            def root(b, q):
                wait_for(pool, var_ready, nth(b, "h", q))
                pool.tensor_tensor(rstd[:, :], var_eps[:, :], minus_half[:, :], ALU.pow).then_inc(rstd_ready, 1)

            def divide(b, u):
                wait_for(pool, inv_ready, U * b + u + 1, apart=True)
                slot = u % RING
                pool.tensor_scalar(ring[:, slot, :], ring[:, slot, :], rowinv[:, slot:slot + 1], 1.0,
                                   ALU.mult, ALU.mult).then_inc(probs_ready, 1)

            def bias_res(b, half):
                for p in range(2):
                    wait_for(pool, res_loaded[p], DMA * (2 * b + half + 1))
                    bias = bo_sb[:, :].unsqueeze(1).broadcast_to([P, 2, D])
                    pool.tensor_tensor(res[:, p, :, :], res[:, p, :, :], bias, ALU.add).then_inc(res_biased, 1)

            for w, t, loaded in ((Wk, wk_sb, wk_loaded), (Wq, wq_sb, wq_loaded), (Wv, wv_sb, wv_loaded),
                                 (Wo, wo_sb, wo_loaded)):
                pool.dma_start(t[:, :, :], w.rearrange("(c p) n -> p c n", p=P)).then_inc(loaded, DMA)
            pool.memset(minus_half[:, :], -0.5).then_inc(half_ready, 1)
            pool.memset(ident[:, :], 0.0).then_inc(ident_zeroed, 1)
            pool.wait_ge(ident_zeroed, 1)
            pool.affine_select(out=ident[:, :], in_=ident[:, :], compare_op=ALU.not_equal, fill=1.0, base=0,
                               pattern=[[-1, P]], channel_multiplier=1).then_inc(ident_ready, 1)
            pool.wait_ge(ident_ready, 1)
            for t in range(HG):
                add = pool.tensor_copy(adder[t * HD:(t + 1) * HD, :], ident[t * HD:(t + 1) * HD, t * HD:(t + 1) * HD])
            add.then_inc(adder_ready, 1)
            pool.wait_ge(adder_ready, 1)
            pool.wait_ge(half_ready, 1)
            for q in range(QUARTERS):
                root(0, q)
            for i in range(TILES):
                pool.wait_ge(adj_loaded[i], DMA)
                pool.tensor_scalar(mask[:, i, :], mask[:, i, :], -1.0, -1e9, ALU.add, ALU.mult).then_inc(mask_ready, 1)
            pool.wait_ge(biases_loaded, 4 * DMA)

            def batch(b, first=False, last=False):
                for u in range(U):
                    divide(b, u)
                    at = u - AHEAD + 1
                    if at in STATS_AT and not last:
                        root(b + 1, STATS_AT[at])
                    if u == QT and not first:
                        bias_res(b - 1, 1)
                    if u == CU + QT:
                        bias_res(b, 0)

            batch(0, first=True)
            with pool.Fori(1, B - 1) as b:
                batch(b)
            batch(B - 1, last=True)
            bias_res(B - 1, 1)


_INS = ["x", "adj", "L0_gnn_Wq", "L0_gnn_bq", "L0_gnn_Wk", "L0_gnn_bk", "L0_gnn_Wv", "L0_gnn_bv", "L0_gnn_Wo", "L0_gnn_bo"]


def kernel(**inputs):
    import numpy as _np
    import concourse.bacc as _bacc
    from concourse import mybir as _mybir
    from concourse.bass_utils import run_bass_kernel_spmd as _run

    nc = _bacc.Bacc("TRN2", target_bir_lowering=False, num_devices=1)
    arrays, args = {}, []
    for name in _INS:
        a = _np.ascontiguousarray(inputs[name])
        arrays[f"in_{name}_dram"] = a
        args.append(nc.dram_tensor(f"in_{name}_dram", a.shape, _mybir.dt.from_np(a.dtype), kind="ExternalInput").ap())
    shape = arrays["in_x_dram"].shape
    args.append(nc.dram_tensor("out_0_dram", shape, _mybir.dt.float32, kind="ExternalOutput").ap())
    graph_attention(nc, *args)
    r = _run(nc, [arrays], core_ids=[0])
    return r.results[0]["out_0_dram"]
```

```python
from contextlib import ExitStack

import concourse.bass as bass
from concourse import mybir

F32 = mybir.dt.float32
F32R = mybir.dt.float32r
ALU = mybir.AluOpType
ACT = mybir.ActivationFunctionType

P = 128
DMA = 16


def graph_attention(nc, x, adj, Wq, bq, Wk, bk, Wv, bv, Wo, bo, out):
    B, N, D = x.shape
    HD = 32
    HG = P // HD
    G = D // P
    TILES = N // P
    QH = 512
    HALVES = N // QH
    QT = QH // P
    CHUNKS = G * HALVES
    CU = HG * QT
    U = CHUNKS * CU
    QUARTERS = N // 256
    AHEAD = 5
    RING = 8
    HEADS = U // QT
    SCALE = -float(HD) ** -0.5
    REP = 2 * HG * DMA

    PREP = [("q", 1, (1, 3), 0), ("s", 3, (5,), -1), ("k", (1, 0), (7, 9), 0), ("o", (1, 0), (11, 12), -1),
            ("k", (1, 1), (13, 15), 0), ("q", 2, (17, 19), 0), ("s", 0, (21,), 0), ("o", (1, 1), (22, 23), -1),
            ("v", (1, 0), (24, 25), 0), ("q", 3, (27, 29), 0), ("v", (1, 1), (31, 33), 0),
            ("h", 0, (34,), 1), ("h", 1, (35,), 1), ("s", 1, (36,), 0), ("h", 2, (37,), 1), ("h", 3, (38,), 1),
            ("k", (0, 0), (39, 40), 1), ("v", (0, 0), (42, 43), 1), ("q", 0, (44, 45), 1),
            ("v", (0, 1), (47, 48), 1), ("k", (0, 1), (49, 51), 1), ("s", 2, (53,), 0), ("o", (0, 0), (55, 57), 0),
            ("o", (0, 1), (59, 61), 0)]
    FIRST = [("h", 0), ("h", 1), ("k", (0, 0)), ("h", 2), ("h", 3), ("q", 0), ("k", (0, 1)),
             ("v", (0, 0)), ("v", (0, 1)), ("v", (1, 0))]
    FIRST_SPLIT = {("k", (0, 0)): RING - 3, ("q", 0): RING - 2, ("k", (0, 1)): RING - 1}

    NORM = [(11, 13, 14, 15), (17, 18, 19, 21), (22, 23, 25, 27), (28, 29, 31, 32)]

    NTH = {"h": {q: q + 1 for q in range(QUARTERS)},
           "qk": {("k", (0, 0)): 1, ("q", 0): 2, ("k", (0, 1)): 3, ("q", 1): 4, ("k", (1, 0)): 5, ("k", (1, 1)): 6,
                  ("q", 2): 7, ("q", 3): 8},
           "s": {c: c + 1 for c in range(CHUNKS)},
           "v": {(0, 0): 1, (0, 1): 2, (1, 0): 3, (1, 1): 4},
           "o": {(0, 0): 1, (0, 1): 2, (1, 0): 3, (1, 1): 4}}
    OPERANDS_FOR_CHUNK = [3, 4, 7, 8]

    def nth(b, what, arg):
        if what in "qk":
            return 8 * b + NTH["qk"][(what, arg)]
        return 4 * b + NTH[what][arg]

    def prep_at(s, first, last):
        return [(w, a, n, at.index(s), len(at)) for w, a, at, n in PREP
                if s in at and not (first and (n < 0 or n == 0 and (w, a) in FIRST) or last and n > 0)]

    def prep_out_at(s, first, last):
        return [(w, a, n) for w, a, n, i, count in prep_at(s - 1, first, last) if i == count - 1]

    AFTER = [(w, a) for w, a, _, n in PREP if n < 0]

    def wait_for(eng, semaphore, count, apart=False):
        if isinstance(count, int) and count <= 0:
            return
        eng.wait_ge(semaphore, count)
        if apart:
            eng.sem_inc(wait_passed, 1)

    with ExitStack() as ctx:
        def sb(name, shape, dt=F32):
            return ctx.enter_context(nc.sbuf_tensor(name, shape, dt))

        def ps(name, shape):
            return ctx.enter_context(nc.psum_tensor(name, shape, F32))

        def sem(name):
            return ctx.enter_context(nc.semaphore(name))

        mask = sb("mask", [P, TILES, N])
        k4 = [sb(f"k4_{g}", [P, HG, N], F32R) for g in range(G)]
        q4 = [sb(f"q4_{i}", [P, HG, QH], F32R) for i in range(2)]
        split = [sb(f"split_{i}", [P, 2, QH], F32R) for i in range(2)]
        v_sb = [sb(f"v_{g}", [P, TILES, P]) for g in range(G)]
        ring = sb("ring", [P, RING, N])
        probs_t = sb("probs_t", [P, 2, TILES, QH])
        parts_sb = sb("parts_sb", [P, HG, QH])
        adder = sb("adder", [P, HD])
        xh = sb("xh", [P, QUARTERS, 2, D])
        h_t = sb("h_t", [P, G, N])
        attn_t = sb("attn_t", [P, HALVES + 1, QH])
        res = sb("res", [P, 2, 2, D])
        wq_sb, wk_sb, wv_sb, wo_sb = (sb(n, [P, G, D]) for n in ("wq_sb", "wk_sb", "wv_sb", "wo_sb"))
        bq_sb, bk_sb = sb("bq_sb", [P, G]), sb("bk_sb", [P, G])
        bv_sb, bo_sb = sb("bv_sb", [P, D]), sb("bo_sb", [P, D])
        ident = sb("ident", [P, P])
        rowmin, rowsum, rowinv = (sb(n, [P, RING]) for n in ("rowmin", "rowsum", "rowinv"))
        stats = sb("stats", [P, QUARTERS, 2, 6])
        moments = sb("moments", [P, QUARTERS, 2, 2])
        var_eps, rstd = (sb(n, [P, QUARTERS, 2]) for n in ("var_eps", "rstd"))
        minus_half = sb("minus_half", [P, 2])

        scores = [ps(f"scores_{i}", [P, N]) for i in range(2)]
        block_t = [ps(f"block_t_{i}", [P, QT * P]) for i in range(2)]
        parts = ps("parts", [P, QH])
        prep = ps("prep", [P, QH])
        first_banks = [prep, block_t[0], block_t[1], parts]
        last_banks = dict(zip(AFTER, (prep, block_t[0], block_t[1])))

        adj_loaded = [sem(f"adj_loaded_{i}") for i in range(TILES)]
        wk_loaded, wq_loaded, wv_loaded, wo_loaded = (sem(f"w{n}_loaded") for n in "kqvo")
        qk_biases_loaded, vo_biases_loaded = sem("qk_biases_loaded"), sem("vo_biases_loaded")
        x_loaded = [sem(f"x_loaded_{i}") for i in range(QUARTERS)]
        res_loaded = [sem(f"res_loaded_{i}") for i in range(2)]
        y_stored = [sem(f"y_stored_{i}") for i in range(2)]
        ident_zeroed, ident_ready = sem("ident_zeroed"), sem("ident_ready")
        adder_ready = sem("adder_ready")
        half_ready, mask_ready, wq_scaled = sem("half_ready"), sem("mask_ready"), sem("wq_scaled")
        bn_done, aggr_done, var_ready, rstd_ready = (sem(n) for n in ("bn_done", "aggr_done", "var_ready", "rstd_ready"))
        xn_ready = sem("xn_ready")
        product = {"h": sem("h_product"), "qk": sem("qk_product"), "v": sem("v_product"), "o": sem("o_product"),
                   "s": sem("s_product")}
        h_ready, hi_ready, split_ready, v_ready, y_ready = (
            sem(n) for n in ("h_ready", "hi_ready", "split_ready", "v_ready", "y_ready"))
        spread_done = [sem(f"spread_done_{i}") for i in range(2)]
        first_spread = [sem(f"first_spread_{j}") for j in range(HG)]
        res_biased = sem("res_biased")
        scores_ready = sem("scores_ready")
        masked_ready = sem("masked_ready")
        exp_ready = sem("exp_ready")
        inv_ready = sem("inv_ready")
        probs_ready = sem("probs_ready")
        block_ready = [sem(f"block_ready_{i}") for i in range(2)]
        block_taken = [sem(f"block_taken_{i}") for i in range(2)]
        half_used = [sem(f"half_used_{i}") for i in range(2)]
        parts_taken = sem("parts_taken")
        attn_ready = sem("attn_ready")
        wait_passed = sem("wait_passed")

        def unit(u):
            return u // (HALVES * CU), u // CU % HALVES, u // QT % HG, u % QT

        def quarter_view(t, b, q):
            return t[b, q * 256:(q + 1) * 256, :].rearrange("(t p) d -> p t d", p=P)

        def is_first(b, what, arg):
            return isinstance(b, int) and b == 0 and (what, arg) in FIRST_SPLIT

        def split_for(b, what, arg):
            if is_first(b, what, arg):
                return ring[:, FIRST_SPLIT[(what, arg)], :].rearrange("p (t n) -> p t n", n=QH).bitcast(F32R)
            return split[turn(what, arg)][:, :, :]

        def turn(what, arg):
            return NTH["qk"][(what, arg)] % 2

        def spreads(b, count, i):
            return REP * (4 * b + (count + i) // 2 - (len(FIRST_SPLIT) + i) // 2)

        def normalise_x(eng, b, q):
            wait_for(eng, rstd_ready, nth(b, "h", q), apart=True)
            for t in range(2):
                ts = eng.tensor_scalar(xh[:, q, t, :], xh[:, q, t, :], moments[:, q, t, 0:1], rstd[:, q, t:t + 1],
                                       ALU.subtract, ALU.mult)
            ts.then_inc(xn_ready, 1)

        block = ctx.enter_context(nc.Block())

        @block.sync
        def _(sp):
            def spread_head(b, what, arg, j, done):
                rows = split_for(b, what, arg)[j * HD:(j + 1) * HD, :, :].bitcast(F32)
                for r in range(2):
                    if what == "k":
                        dst = k4[arg[0]][r * 2 * HD:(r + 1) * 2 * HD, j, arg[1] * QH:(arg[1] + 1) * QH]
                        src = rows[:, r, :].unsqueeze(1).broadcast_to([HD, 2, QH])
                    else:
                        dst = q4[arg % 2][r * 2 * HD:(r + 1) * 2 * HD, j, :]
                        src = rows
                    sp.dma_start(dst.bitcast(F32), src).then_inc(done, DMA)

            def spread(b, what, arg):
                wait_for(sp, split_ready, nth(b, what, arg), apart=True)
                back = CU * (arg - 1) if what == "q" else HALVES * CU * (arg[0] - 1)
                wait_for(sp, scores_ready, U * b + back, apart=True)
                for j in range(HG):
                    spread_head(b, what, arg, j, spread_done[turn(what, arg)])

            def load_x(b, q):
                wait_for(sp, product["h"], nth(b - 1, "h", q), apart=True)
                sp.dma_start(xh[:, q, :, :], quarter_view(x, b, q)).then_inc(x_loaded[q], DMA)

            def load_res(b, half):
                for p in range(2):
                    wait_for(sp, y_stored[p], DMA * (2 * b + half), apart=True)
                    sp.dma_start(res[:, p, :, :], quarter_view(x, b, 2 * half + p)).then_inc(res_loaded[p], DMA)

            def store_y(b, half, p):
                wait_for(sp, y_ready, nth(b, "o", (half, p)), apart=True)
                sp.dma_start(quarter_view(out, b, 2 * half + p), res[:, p, :, :]).then_inc(y_stored[p], DMA)

            def load_weights(w, t, loaded):
                sp.dma_start(t[:, :, :], w.rearrange("(c p) n -> p c n", p=P)).then_inc(loaded, DMA)

            def load_adj(half):
                for i in range(half * QT, (half + 1) * QT):
                    sp.dma_start(mask[:, i, :], adj[i * P:(i + 1) * P, :]).then_inc(adj_loaded[i], DMA)

            for q in range(QUARTERS):
                load_x(0, q)
            load_weights(Wk, wk_sb, wk_loaded)
            load_weights(Wq, wq_sb, wq_loaded)
            for v, t in ((bq, bq_sb), (bk, bk_sb)):
                sp.dma_start(t[:, :], v.rearrange("(g p) -> p g", p=P),
                             allow_slow_non_contiguous=True).then_inc(qk_biases_loaded, DMA)
            load_weights(Wv, wv_sb, wv_loaded)
            for v, t in ((bv, bv_sb), (bo, bo_sb)):
                sp.dma_start(t[:, :], v.partition_broadcast(P)).then_inc(vo_biases_loaded, DMA)
            load_adj(0)
            for heads in ((0, 1), (2, 3)):
                for what, arg in FIRST_SPLIT:
                    if heads[0] == 0:
                        wait_for(sp, split_ready, nth(0, what, arg))
                    for j in heads:
                        spread_head(0, what, arg, j, first_spread[j])
            load_adj(1)
            load_weights(Wo, wo_sb, wo_loaded)

            def batch(b, first=False, last=False):
                spread(b, "q", 1)
                if not last:
                    for q in range(QUARTERS):
                        load_x(b + 1, q)
                spread(b, "k", (1, 0))
                if not first:
                    store_y(b - 1, 1, 0)
                spread(b, "k", (1, 1))
                spread(b, "q", 2)
                if not first:
                    store_y(b - 1, 1, 1)
                load_res(b, 0)
                spread(b, "q", 3)
                if not last:
                    spread(b + 1, "k", (0, 0))
                    spread(b + 1, "q", 0)
                    spread(b + 1, "k", (0, 1))
                store_y(b, 0, 0)
                store_y(b, 0, 1)
                load_res(b, 1)

            batch(0, first=True)
            with sp.Fori(1, B - 1) as b:
                batch(b)
            batch(B - 1, last=True)
            store_y(B - 1, 1, 0)
            store_y(B - 1, 1, 1)
            for p in range(2):
                sp.wait_ge(y_stored[p], DMA * 2 * B)

        @block.tensor
        def _(pe):
            def prep_product(b, what, arg, i=0, count=1, bank=prep):
                if what == "h":
                    wait_for(pe, xn_ready, nth(b, "h", arg))
                    for c in range(G):
                        for t in range(2):
                            mm = pe.transpose(bank[:, (2 * c + t) * P:(2 * c + t + 1) * P],
                                              xh[:, arg, t, c * P:(c + 1) * P], ident[:, :])
                elif what in "qk":
                    g, half = divmod(arg, HALVES) if what == "q" else arg
                    w = wq_sb if what == "q" else wk_sb
                    for c in range(i * G // count, (i + 1) * G // count):
                        mm = pe.matmul(bank[:, :], w[:, c, g * P:(g + 1) * P], h_t[:, c, half * QH:(half + 1) * QH],
                                       start=(c == 0), stop=(c == G - 1))
                elif what == "v":
                    g, half = arg
                    for t in range(i * QT // count, (i + 1) * QT // count):
                        at = half * QH + t * P
                        for c in range(G):
                            mm = pe.matmul(bank[:, t * P:(t + 1) * P], h_t[:, c, at:at + P],
                                           wv_sb[:, c, g * P:(g + 1) * P], start=(c == 0), stop=(c == G - 1))
                elif what == "s":
                    wait_for(pe, parts_taken, HEADS * b + HG * (arg + 1))
                    for j in range(HG):
                        mm = pe.matmul(bank[j * HD:(j + 1) * HD, :], adder[:, :], parts_sb[:, j, :], start=True, stop=True)
                else:
                    half, pair = arg
                    if isinstance(b, int) and b == 0:
                        pe.wait_ge(wo_loaded, DMA)
                    wait_for(pe, attn_ready, nth(b, "s", HALVES + half))
                    for t in range(i * 2 // count, (i + 1) * 2 // count):
                        at = (2 * pair + t) * P
                        for g in range(G):
                            mm = pe.matmul(bank[:, t * D:(t + 1) * D], attn_t[:, half if g == 0 else HALVES, at:at + P],
                                           wo_sb[:, g, :], start=(g == 0), stop=(g == G - 1))
                if i == count - 1:
                    mm.then_inc(product["qk" if what in "qk" else what], 1)

            def prep_bank_free(b, what, arg):
                free = {"h": h_ready, "q": split_ready, "k": split_ready, "v": v_ready, "o": y_ready,
                        "s": attn_ready}[what]
                wait_for(pe, free, nth(b, what, arg))

            def score(b, u):
                g, half, j, qt = unit(u)
                if u % CU == 0:
                    for i in range(2):
                        wait_for(pe, spread_done[i], spreads(b, OPERANDS_FOR_CHUNK[u // CU], i))
                if isinstance(b, int) and b == 0 and u < CU and qt == 0:
                    pe.wait_ge(first_spread[j], 2 * len(FIRST_SPLIT) * DMA)
                wait_for(pe, masked_ready, U * b + u - 1)
                for n in range(N // QH):
                    mm = pe.matmul(scores[u % 2][:, n * QH:(n + 1) * QH], q4[half][:, j, qt * P:(qt + 1) * P],
                                   k4[g][:, j, n * QH:(n + 1) * QH], start=True, stop=True)
                mm.then_inc(scores_ready, 1)

            def transposes(b, u):
                wait_for(pe, probs_ready, U * b + u + 1)
                for i in (1, 0):
                    wait_for(pe, block_taken[i], U * b + u)
                    for t in range(QT):
                        at = (i * QT + t) * P
                        mm = pe.transpose(block_t[i][:, t * P:(t + 1) * P], ring[:, u % RING, at:at + P], ident[:, :])
                    mm.then_inc(block_ready[i], 1)

            def attend(b, n, i):
                g, half, j, _ = unit(QT * n)
                wait_for(pe, block_taken[i], U * b + QT * (n + 1))
                if i == 0:
                    wait_for(pe, v_ready, nth(b, "v", (g, 1)))
                    wait_for(pe, parts_taken, HEADS * b + n)
                for t in range(QT):
                    mm = pe.matmul(parts[t * HD:(t + 1) * HD, :], v_sb[g][:, i * QT + t, j * HD:(j + 1) * HD],
                                   probs_t[:, j % 2, i * QT + t, :], start=(i == 0), stop=(i == 1))
                mm.then_inc(half_used[i], 1)

            pe.wait_ge(ident_ready, 1)
            for n, (what, arg) in enumerate(FIRST):
                if n >= len(first_banks):
                    prep_bank_free(0, *FIRST[n - len(first_banks)])
                if what != "h":
                    half = 0 if what == "q" else arg[1]
                    pe.wait_ge(h_ready, QUARTERS // HALVES * (half + 1))
                if (what, arg) == ("k", (0, 0)):
                    pe.wait_ge(wk_loaded, DMA)
                if (what, arg) == ("v", (0, 0)):
                    pe.wait_ge(wv_loaded, DMA)
                if (what, arg) == ("q", 0):
                    pe.wait_ge(wq_scaled, 1)
                prep_product(0, what, arg, bank=first_banks[n % len(first_banks)])
            pe.wait_ge(adder_ready, 1)
            for u in range(AHEAD):
                score(0, u)
            pe.wait_ge(v_ready, nth(0, *FIRST[-1]))

            def batch(b, first=False, last=False):
                before = (0, *FIRST[-1]) if first else (b - 1, "o", (0, 1))
                for s in range(U):
                    if s + AHEAD < U:
                        score(b, s + AHEAD)
                    elif not last:
                        score(b + 1, s + AHEAD - U)
                    transposes(b, s)
                    if s % QT in (0, 2):
                        if s >= QT:
                            attend(b, s // QT - 1, s % QT // 2)
                        elif not first:
                            attend(b - 1, HEADS - 1, s % QT // 2)
                    for what, arg, n, i, count in prep_at(s, first, last):
                        if i == 0:
                            prep_bank_free(*before)
                        prep_product(b + n, what, arg, i, count)
                        before = b + n, what, arg

            batch(0, first=True)
            with pe.Fori(1, B - 1) as b:
                batch(b)
            batch(B - 1, last=True)
            attend(B - 1, HEADS - 1, 0)
            attend(B - 1, HEADS - 1, 1)
            before = (B - 1, "o", (0, 1))
            for what, arg in AFTER:
                if what == "s":
                    prep_bank_free(*before)
                prep_product(B - 1, what, arg, bank=last_banks[what, arg])

        @block.vector
        def _(dve):
            def norm_step(b, q, step):
                if step < 2:
                    if step == 0:
                        wait_for(dve, x_loaded[q], DMA * (b + 1))
                    bn = dve.bn_stats(stats[:, q, step, :], xh[:, q, step, :])
                    if step == 1:
                        bn.then_inc(bn_done, 1)
                elif step == 2:
                    wait_for(dve, bn_done, nth(b, "h", q), apart=True)
                    for t in range(2):
                        aggr = dve.bn_aggr(moments[:, q, t, :], stats[:, q, t, :])
                    aggr.then_inc(aggr_done, 1)
                else:
                    wait_for(dve, aggr_done, nth(b, "h", q))
                    dve.tensor_scalar(var_eps[:, q, :], moments[:, q, :, 1], 1e-5, None, ALU.add).then_inc(var_ready, 1)

            def prep_out(b, what, arg, bank=prep):
                if what in "qk":
                    g = arg // HALVES if what == "q" else arg[0]
                    wait_for(dve, hi_ready, nth(b, what, arg))
                    parts_of = split_for(b, what, arg)
                    dve.scalar_tensor_tensor(out=parts_of[:, 1, :], in0=bank[:, :],
                                             scalar=(bq_sb if what == "q" else bk_sb)[:, g:g + 1],
                                             in1=parts_of[:, 0, :].bitcast(F32),
                                             op0=ALU.add, op1=ALU.subtract).then_inc(split_ready, 1)
                elif what == "v":
                    g, half = arg
                    wait_for(dve, product["v"], nth(b, what, arg))
                    wait_for(dve, half_used[1], HEADS * b + HEADS // G * (g - 1))
                    bias = bv_sb[:, g * P:(g + 1) * P].unsqueeze(1).broadcast_to([P, QT, P])
                    dve.tensor_tensor(v_sb[g][:, half * QT:(half + 1) * QT, :],
                                      bank[:, :].rearrange("p (t n) -> p t n", n=P), bias, ALU.add).then_inc(v_ready, 1)
                elif what == "o":
                    half, pair = arg
                    wait_for(dve, product["o"], nth(b, what, arg))
                    wait_for(dve, res_biased, nth(b, what, arg))
                    dve.tensor_tensor(res[:, pair, :, :], bank[:, :].rearrange("p (t n) -> p t n", n=D),
                                      res[:, pair, :, :], ALU.add).then_inc(y_ready, 1)

            def mask_and_min(b, u):
                g, half, j, qt = unit(u)
                dve.wait_ge(mask_ready, half * QT + qt + 1)
                if isinstance(b, int) and b == 0 and u == RING - len(FIRST_SPLIT):
                    for done in first_spread:
                        dve.wait_ge(done, 2 * len(FIRST_SPLIT) * DMA)
                wait_for(dve, block_ready[1], U * b + u + 1 - RING)
                wait_for(dve, scores_ready, U * b + u + 1, apart=True)
                slot = u % RING
                dve.tensor_tensor_reduce(ring[:, slot, :], scores[u % 2][:, :], mask[:, half * QT + qt, :], 1.0, 3.4e38,
                                         ALU.add, ALU.min, rowmin[:, slot:slot + 1]).then_inc(masked_ready, 1)

            def invert_sum(b, u):
                wait_for(dve, exp_ready, U * b + u + 1)
                slot = u % RING
                dve.reciprocal(rowinv[:, slot:slot + 1], rowsum[:, slot:slot + 1]).then_inc(inv_ready, 1)

            def take_block(b, u):
                g, half, j, qt = unit(u)
                wait_for(dve, block_ready[0], U * b + u + 1)
                if u % QT == 0:
                    wait_for(dve, half_used[0], HEADS * b + u // QT - 1)
                dve.tensor_copy(probs_t[:, j % 2, 0:QT, qt * P:(qt + 1) * P],
                                block_t[0][:, :].rearrange("p (t n) -> p t n", n=P)).then_inc(block_taken[0], 1)

            for pair in ((0, 1), (2, 3)):
                for q in pair:
                    for step in range(4):
                        norm_step(0, q, step)
                for q in pair:
                    normalise_x(dve, 0, q)
                if pair[0] == 0:
                    dve.wait_ge(wq_loaded, DMA)
                    dve.wait_ge(qk_biases_loaded, 2 * DMA)
                    dve.tensor_scalar(bq_sb[:, :], bq_sb[:, :], SCALE, None, ALU.mult)
                    dve.tensor_scalar(wq_sb[:, :, :], wq_sb[:, :, :], SCALE, None, ALU.mult).then_inc(wq_scaled, 1)
            dve.wait_ge(wq_scaled, 1)
            dve.wait_ge(vo_biases_loaded, 2 * DMA)
            for n, (what, arg) in enumerate(FIRST):
                prep_out(0, what, arg, first_banks[n % len(first_banks)])
            for u in range(AHEAD):
                mask_and_min(0, u)
                if u >= 2:
                    invert_sum(0, u - 2)
            invert_sum(0, AHEAD - 2)

            def batch(b, first=False, last=False):
                for s in range(U):
                    busy = prep_out_at(s, first, last)
                    for what, arg, n in busy:
                        if what in "vo":
                            prep_out(b + n, what, arg)
                    if s + AHEAD < U:
                        mask_and_min(b, s + AHEAD)
                    elif not last:
                        mask_and_min(b + 1, s + AHEAD - U)
                    take_block(b, s)
                    if s + AHEAD - 1 < U:
                        invert_sum(b, s + AHEAD - 1)
                    elif not last:
                        invert_sum(b + 1, s + AHEAD - 1 - U)
                    for what, arg, n in busy:
                        if what in "qk":
                            prep_out(b + n, what, arg)
                    if not last:
                        for q, steps in enumerate(NORM):
                            if s in steps:
                                norm_step(b + 1, q, steps.index(s))

            batch(0, first=True)
            with dve.Fori(1, B - 1) as b:
                batch(b)
            batch(B - 1, last=True)
            for what, arg in AFTER:
                prep_out(B - 1, what, arg, last_banks[what, arg])

        @block.scalar
        def _(act):
            def prep_out(b, what, arg, bank=prep):
                if what == "h":
                    wait_for(act, product["h"], nth(b, what, arg))
                    act.activation(h_t[:, :, arg * 256:(arg + 1) * 256], bank[:, :].rearrange("p (c n) -> p c n", c=G),
                                   ACT.Relu).then_inc(h_ready, 1)
                elif what in "qk":
                    g = arg // HALVES if what == "q" else arg[0]
                    wait_for(act, product["qk"], nth(b, what, arg))
                    wait_for(act, spread_done[turn(what, arg)], spreads(b, NTH["qk"][(what, arg)] - 2, turn(what, arg)))
                    act.activation(split_for(b, what, arg)[:, 0, :], bank[:, :], ACT.Identity,
                                   bias=(bq_sb if what == "q" else bk_sb)[:, g:g + 1]).then_inc(hi_ready, 1)
                elif what == "s":
                    wait_for(act, product["s"], nth(b, what, arg))
                    act.copy(attn_t[:, min(arg, HALVES), :], bank[:, :]).then_inc(attn_ready, 1)

            def exponential(b, u):
                wait_for(act, masked_ready, U * b + u + 1)
                slot = u % RING
                act.activation(ring[:, slot, :], ring[:, slot, :], ACT.Exp, bias=rowmin[:, slot:slot + 1], scale=-1.0,
                               accum_out=rowsum[:, slot:slot + 1]).then_inc(exp_ready, 1)

            def take_block(b, u):
                g, half, j, qt = unit(u)
                wait_for(act, block_ready[1], U * b + u + 1)
                if u % QT == 0:
                    wait_for(act, half_used[1], HEADS * b + u // QT - 1)
                act.copy(probs_t[:, j % 2, QT:TILES, qt * P:(qt + 1) * P],
                         block_t[1][:, :].rearrange("p (t n) -> p t n", n=P)).then_inc(block_taken[1], 1)

            def take_parts(b, n):
                wait_for(act, half_used[1], HEADS * b + n + 1)
                if n % HG == 0:
                    wait_for(act, product["s"], CHUNKS * b + n // HG)
                act.copy(parts_sb[:, n % HG, :], parts[:, :]).then_inc(parts_taken, 1)

            for n, (what, arg) in enumerate(FIRST):
                if what == "k":
                    act.wait_ge(qk_biases_loaded, 2 * DMA)
                if what == "q":
                    act.wait_ge(wq_scaled, 1)
                prep_out(0, what, arg, first_banks[n % len(first_banks)])
            for u in range(AHEAD):
                exponential(0, u)

            def batch(b, first=False, last=False):
                for s in range(U):
                    for what, arg, n in prep_out_at(s, first, last):
                        prep_out(b + n, what, arg)
                    if s % QT == QT - 1:
                        if s >= QT:
                            take_parts(b, s // QT - 1)
                        elif not first:
                            take_parts(b - 1, HEADS - 1)
                    take_block(b, s)
                    if s + AHEAD < U:
                        exponential(b, s + AHEAD)
                    elif not last:
                        exponential(b + 1, s + AHEAD - U)

            batch(0, first=True)
            with act.Fori(1, B - 1) as b:
                batch(b)
            batch(B - 1, last=True)
            take_parts(B - 1, HEADS - 1)
            for what, arg in AFTER:
                prep_out(B - 1, what, arg, last_banks[what, arg])

        @block.gpsimd
        def _(pool):
            def root(b, q):
                wait_for(pool, var_ready, nth(b, "h", q))
                pool.tensor_tensor(rstd[:, q, :], var_eps[:, q, :], minus_half[:, :], ALU.pow).then_inc(rstd_ready, 1)

            def divide(b, u):
                wait_for(pool, inv_ready, U * b + u + 1, apart=True)
                slot = u % RING
                pool.tensor_scalar(ring[:, slot, :], ring[:, slot, :], rowinv[:, slot:slot + 1], 1.0,
                                   ALU.mult, ALU.mult).then_inc(probs_ready, 1)

            def bias_res(b, half):
                for p in range(2):
                    wait_for(pool, res_loaded[p], DMA * (2 * b + half + 1))
                    bias = bo_sb[:, :].unsqueeze(1).broadcast_to([P, 2, D])
                    pool.tensor_tensor(res[:, p, :, :], res[:, p, :, :], bias, ALU.add).then_inc(res_biased, 1)

            def make_mask(i):
                pool.wait_ge(adj_loaded[i], DMA)
                pool.tensor_scalar(mask[:, i, :], mask[:, i, :], -1.0, -1e9, ALU.add, ALU.mult).then_inc(mask_ready, 1)

            pool.memset(minus_half[:, :], -0.5).then_inc(half_ready, 1)
            pool.memset(ident[:, :], 0.0).then_inc(ident_zeroed, 1)
            pool.wait_ge(ident_zeroed, 1)
            pool.affine_select(out=ident[:, :], in_=ident[:, :], compare_op=ALU.not_equal, fill=1.0, base=0,
                               pattern=[[-1, P]], channel_multiplier=1).then_inc(ident_ready, 1)
            pool.wait_ge(ident_ready, 1)
            for t in range(HG):
                add = pool.tensor_copy(adder[t * HD:(t + 1) * HD, :], ident[t * HD:(t + 1) * HD, t * HD:(t + 1) * HD])
            add.then_inc(adder_ready, 1)
            pool.wait_ge(adder_ready, 1)
            pool.wait_ge(half_ready, 1)
            for q in range(QUARTERS):
                root(0, q)
            for i in range(QT):
                make_mask(i)
            pool.wait_ge(vo_biases_loaded, 2 * DMA)

            def batch(b, first=False, last=False):
                for u in range(U):
                    divide(b, u)
                    if first and u % 2 and u // 2 < TILES - QT:
                        make_mask(QT + u // 2)
                    for q, steps in enumerate(NORM):
                        if u == steps[-1] + AHEAD - 1 and not last:
                            root(b + 1, q)
                            normalise_x(pool, b + 1, q)
                    if u == QT and not first:
                        bias_res(b - 1, 1)
                    if u == 2 * CU:
                        bias_res(b, 0)

            batch(0, first=True)
            with pool.Fori(1, B - 1) as b:
                batch(b)
            batch(B - 1, last=True)
            bias_res(B - 1, 1)


_INS = ["x", "adj", "L0_gnn_Wq", "L0_gnn_bq", "L0_gnn_Wk", "L0_gnn_bk", "L0_gnn_Wv", "L0_gnn_bv", "L0_gnn_Wo", "L0_gnn_bo"]


def kernel(**inputs):
    import numpy as _np
    import concourse.bacc as _bacc
    from concourse import mybir as _mybir
    from concourse.bass_utils import run_bass_kernel_spmd as _run

    nc = _bacc.Bacc("TRN2", target_bir_lowering=False, num_devices=1)
    arrays, args = {}, []
    for name in _INS:
        a = _np.ascontiguousarray(inputs[name])
        arrays[f"in_{name}_dram"] = a
        args.append(nc.dram_tensor(f"in_{name}_dram", a.shape, _mybir.dt.from_np(a.dtype), kind="ExternalInput").ap())
    shape = arrays["in_x_dram"].shape
    args.append(nc.dram_tensor("out_0_dram", shape, _mybir.dt.float32, kind="ExternalOutput").ap())
    graph_attention(nc, *args)
    r = _run(nc, [arrays], core_ids=[0])
    return r.results[0]["out_0_dram"]
```
